# Optimizing a Trainium2 kernel written in Bass

```python
import numpy as np
import jax
import jax.numpy as jnp

def _softmax(x, axis=-1):
    return jax.nn.softmax(x, axis=axis)
def _gelu(x):
    return jax.nn.gelu(x, approximate=True)
def _silu(x):
    return jax.nn.silu(x)
def _sigmoid(x):
    return jax.nn.sigmoid(x)
def _layernorm(x, axis=-1, eps=1e-5):
    m = jnp.mean(x, axis=axis, keepdims=True)
    v = jnp.var(x, axis=axis, keepdims=True)
    return (x - m) / jnp.sqrt(v + eps)
def _scatter_add(tgt, idx, src, axis=0):
    return tgt.at[idx].add(src)
def _segment_sum(src, seg, n):
    return jax.ops.segment_sum(src, seg, n)

kernel_name = 'mk_adj_resnorm_d1_adj_256_f7d502'

def setup_inputs(seed: int = 0):
    np.random.seed(seed)
    _w = jnp.asarray
    def _rec_inputs():
        import jax
        import jax.numpy as jnp
        _gk = jax.random.key(seed)
        x = -0.0005146 + 1 * jax.random.normal(jax.random.fold_in(_gk, 1), (8, 2048, 256), jnp.float32)
        _a = jax.random.bernoulli(jax.random.fold_in(_gk, 2), 0.00195312, (8, 2048, 2048))
        adj = _a.astype(jnp.int32)
        return x, adj
    x, adj = _rec_inputs()
    def _L0_gnn_setup():
        import jax, jax.numpy as jnp
        import numpy as np
        B, N, C, OUT, S = (4, 2048, 256, 256, 25)
        DENSITY = 0.008
        key = jax.random.key(seed)
        kA, kX, kW = jax.random.split(key, 3)
        A = jax.random.bernoulli(kA, DENSITY, (B, N, N)).astype(jnp.int32)
        X = jax.random.normal(kX, (B, N, C), dtype=jnp.float32)
        W = jax.random.normal(kW, (2 * C, OUT), dtype=jnp.float32) * np.float32(1.0 / np.sqrt(2 * C))
        b = jnp.zeros((OUT,), dtype=jnp.float32)
        return {'A': A, 'X': X, 'W': W, 'b': b}
    _L0_gnn_all = _L0_gnn_setup()
    _L0_gnn_in = {k: v for k, v in _L0_gnn_all.items() if k in ('W', 'b', )}
    del _L0_gnn_all

    return {
        "x": x,
        "adj": adj,
        "L0_gnn_W": _L0_gnn_in["W"],
        "L0_gnn_b": _L0_gnn_in["b"],
    }

def reference(x, adj, L0_gnn_W, L0_gnn_b):
    import jax
    import jax.numpy as jnp
    def _L0_gnn_ref(A, X, W, b):
        import jax, jax.numpy as jnp
        import numpy as np
        B, N, C, OUT, S = (4, 2048, 256, 256, 25)
        DENSITY = 0.008
        mask = A != 0
        neg_inf = jnp.float32(-jnp.inf)
        pri = -jnp.arange(N, dtype=jnp.float32)
        scores = jnp.where(mask, pri, neg_inf)
        vals, idx = jax.lax.top_k(scores, S)
        valid = vals > neg_inf
        feats = jax.vmap(lambda x, i: x[i])(X, idx)
        feats = jnp.where(valid[..., None], feats, neg_inf)
        agg = feats.max(axis=2)
        degree = mask.sum(axis=-1)
        agg = jnp.where((degree <= S)[..., None], jnp.maximum(agg, 0.0), agg)
        h = jnp.concatenate([X, agg], axis=-1)
        out = jax.nn.relu(jnp.einsum('bnf,fo->bno', h, W) + b)
        return out

    x = _layernorm(x + _L0_gnn_ref(adj, x, L0_gnn_W, L0_gnn_b), axis=-1)
    return x


_drawn_inputs = setup_inputs


def setup_inputs(seed=0):
    import zlib

    import numpy as np

    out = dict(_drawn_inputs(seed))
    spreads = {'L0_gnn_b': (0.0, 0.1)}
    factors = {}
    for name, (base, spread) in spreads.items():
        noise = np.random.default_rng([zlib.crc32(name.encode()), seed]).standard_normal(out[name].shape)
        drawn = base * np.exp(spread * noise) if base else spread * noise
        out[name] = jnp.asarray(drawn.astype(out[name].dtype))
    for name, factor in factors.items():
        out[name] = (out[name] * factor).astype(out[name].dtype)
    return out
```

```python
from contextlib import ExitStack

import concourse.bass as bass
from concourse import mybir

P = 128
ALU = mybir.AluOpType
ACT = mybir.ActivationFunctionType
AX_X = mybir.AxisListType.X
F16 = mybir.dt.float16
F32 = mybir.dt.float32
I32 = mybir.dt.int32
U32 = mybir.dt.uint32

S = 25
RANKS = 32
RING = 5
EPS = 1e-5
LOWEST = -3.4028234663852886e38


def graph_layer(nc, x, adj, w, b, out):
    B, N, C = x.shape
    TILES = B * N // P
    K = 2 * C // P
    x_rows = x.rearrange("b n c -> (b n) c")
    x_tiles = x.rearrange("b (t p) c -> (b t) p c", p=P)
    adj_tiles = adj.rearrange("b (t p) m -> (b t) p m", p=P)
    out_tiles = out.rearrange("b (t p) c -> (b t) p c", p=P)

    with ExitStack() as ctx:
        def sb(name, shape, dt=F32):
            return ctx.enter_context(nc.sbuf_tensor(name, shape, dt))

        def ps(name, shape, dt=F32):
            return ctx.enter_context(nc.psum_tensor(name, shape, dt))

        def sem(name):
            return ctx.enter_context(nc.semaphore(name))

        adj_t = sb("adj_t", [P, N], I32)
        x_t = sb("x_t", [P, C])
        descending = sb("descending", [P, N], F16)
        descending_i = sb("descending_i", [P, N], I32)
        key = sb("key", [P, N], F16)
        ranks = sb("ranks", [P, RANKS], F16)
        own_i = sb("own_i", [P, 1], I32)
        own_f = sb("own_f", [P, 1])
        local_i = sb("local_i", [P, 1], I32)
        from_end = sb("from_end", [P, 1])
        valid = sb("valid", [P, S])
        offset = sb("offset", [P, S])
        offset_v = sb("offset_v", [P, S])
        index = sb("index", [P, S], U32)
        floor = sb("floor", [P, 1])
        gathered = sb("gathered", [P, RING, C])
        agg = sb("agg", [P, C])
        identity = sb("identity", [P, P])
        w_t = sb("w_t", [P, K, C])
        b_row = sb("b_row", [1, C])
        ones_row = sb("ones_row", [1, P])
        eps_t = sb("eps_t", [P, 1])
        h_T = sb("h_T", [P, K, P])
        relu_t = sb("relu_t", [P, C])
        y_t = sb("y_t", [P, C])
        stats = sb("stats", [P, 6])
        mean_var = sb("mean_var", [P, 2])
        std = sb("std", [P, 1])
        rstd = sb("rstd", [P, 1])
        shift = sb("shift", [P, 1])
        out_t = sb("out_t", [P, C])
        h_ps = ps("h_ps", [P, K, P])
        lin_ps = ps("lin_ps", [P, C])

        weights_landed = sem("weights_landed")
        consts_ready = sem("consts_ready")
        pool_const = sem("pool_const")
        sp_gate = sem("sp_gate")
        pool_gate = sem("pool_gate")
        adj_landed = sem("adj_landed")
        x_landed = sem("x_landed")
        adj_used = sem("adj_used")
        dve_chain = sem("dve_chain")
        index_ready = sem("index_ready")
        row_landed = [sem(f"row_landed_{r}") for r in range(RING)]
        rows_free = sem("rows_free")
        agg_ready = sem("agg_ready")
        transposed = sem("transposed")
        h_ready = sem("h_ready")
        linear_ready = sem("linear_ready")
        relu_ready = sem("relu_ready")
        var_ready = sem("var_ready")
        std_ready = sem("std_ready")
        scale_ready = sem("scale_ready")
        out_ready = sem("out_ready")
        out_stored = sem("out_stored")
        block = ctx.enter_context(nc.Block())

        @block.sync
        def _(sp):
            sp.dma_start(w_t[:], w.rearrange("(k p) n -> p k n", p=P)).then_inc(weights_landed, 16)
            sp.dma_start(b_row[:], b.rearrange("(a n) -> a n", a=1)).then_inc(weights_landed, 16)
            with sp.Fori(0, TILES) as t:
                sp.wait_ge(adj_used, t + 1)
                sp.sem_inc(sp_gate, 1)
                sp.dma_start(adj_t[:], adj_tiles[bass.ds(t, 1), :, :].rearrange("a p m -> (a p) m")).then_inc(adj_landed, 16)
                sp.wait_ge(scale_ready, t + 1)
                sp.sem_inc(sp_gate, 1)
                sp.dma_start(x_t[:], x_tiles[bass.ds(t, 1), :, :].rearrange("a p m -> (a p) m")).then_inc(x_landed, 16)
                sp.wait_ge(out_ready, t + 1)
                sp.sem_inc(sp_gate, 1)
                sp.dma_start(out_tiles[bass.ds(t, 1), :, :].rearrange("a p m -> (a p) m"), out_t[:]).then_inc(out_stored, 16)
                sp.wait_ge(out_stored, 16 * (t + 1))
                sp.sem_inc(sp_gate, 1)

        @block.gpsimd
        def _(pool):
            nc.gpsimd.iota(descending_i[:], [[-1, N]], base=N, channel_multiplier=0).then_inc(consts_ready, 1)
            nc.gpsimd.iota(own_i[:], [[0, 1]], base=-P, channel_multiplier=1).then_inc(consts_ready, 1)
            nc.gpsimd.memset(ones_row[:], 1.0).then_inc(consts_ready, 1)
            nc.gpsimd.memset(eps_t[:], EPS).then_inc(consts_ready, 1)
            nc.gpsimd.memset(identity[:], 0.0).then_inc(pool_const, 1)
            pool.wait_ge(pool_const, 1)
            nc.gpsimd.affine_select(out=identity[:], in_=identity[:], compare_op=ALU.not_equal, fill=1.0, base=0,
                                    pattern=[[-1, P]], channel_multiplier=1).then_inc(consts_ready, 1)
            with pool.Fori(0, TILES) as t:
                pool.wait_ge(index_ready, t + 1)
                for j in range(S):
                    pool.wait_ge(rows_free, t * S + (j + 1))
                    pool.sem_inc(pool_gate, 1)
                    nc.gpsimd.indirect_dma_start(
                        out=gathered[:, j % RING, :], out_offset=None, in_=x_rows[:, :],
                        in_offset=bass.IndirectOffsetOnAxis(ap=index[:, j:j + 1], axis=0),
                    ).then_inc(row_landed[j % RING], 16)

        @block.vector
        def _(dve):
            dve.wait_ge(consts_ready, 5)
            nc.vector.tensor_copy(descending[:], descending_i[:]).then_inc(dve_chain, 1)
            dve.wait_ge(dve_chain, 1)
            dve.sem_inc(adj_used, 1)
            dve.sem_inc(scale_ready, 1)
            dve.sem_inc(rows_free, RING)
            with dve.Fori(0, TILES) as t:
                count = [0]
                dve.sem_clear(dve_chain)

                def done(ins):
                    count[0] += 1
                    ins.then_inc(dve_chain, 1)
                    dve.wait_ge(dve_chain, count[0])

                done(nc.vector.tensor_scalar(own_i[:], own_i[:], P, None, ALU.add))
                done(nc.vector.tensor_copy(own_f[:], own_i[:]))
                done(nc.vector.tensor_scalar(local_i[:], own_i[:], N - 1, None, ALU.bitwise_and))
                done(nc.vector.tensor_scalar(from_end[:], local_i[:], -1.0, float(N), ALU.mult, ALU.add))
                dve.wait_ge(adj_landed, 16 * (t + 1))
                done(nc.vector.scalar_tensor_tensor(key[:], adj_t[:], 0.0, descending[:], ALU.not_equal, ALU.mult))
                dve.sem_inc(adj_used, 1)
                for r in range(0, RANKS, 8):
                    done(nc.vector.max(ranks[:, r:r + 8], key[:]))
                    if r + 8 < RANKS:
                        done(nc.vector.match_replace(key[:], ranks[:, r:r + 8], key[:], 0.0))
                done(nc.vector.tensor_scalar(valid[:], ranks[:, 0:S], 0.0, None, ALU.is_gt))
                done(nc.vector.tensor_scalar(offset[:], ranks[:, 0:S], -1.0, from_end[:, 0:1], ALU.mult, ALU.add))
                done(nc.vector.tensor_tensor(offset_v[:], offset[:], valid[:], ALU.mult))
                done(nc.vector.tensor_scalar(index[:], offset_v[:], own_f[:, 0:1], None, ALU.add))
                dve.sem_inc(index_ready, 1)
                done(nc.vector.tensor_scalar(floor[:], ranks[:, S:S + 1], 0.0, LOWEST, ALU.is_gt, ALU.mult))
                for j in range(S):
                    dve.wait_ge(row_landed[j % RING], t * (16 * S // RING) + 16 * (j // RING + 1))
                    if j == 0:
                        done(nc.vector.tensor_scalar(agg[:], gathered[:, 0, :], valid[:, 0:1], floor[:, 0:1], ALU.mult, ALU.max))
                    else:
                        done(nc.vector.scalar_tensor_tensor(agg[:], gathered[:, j % RING, :], valid[:, j:j + 1], agg[:],
                                                            ALU.mult, ALU.max))
                    dve.sem_inc(rows_free, 1)
                dve.sem_inc(agg_ready, 1)
                dve.wait_ge(relu_ready, t + 1)
                done(nc.vector.tensor_tensor(y_t[:], relu_t[:], x_t[:], ALU.add))
                done(nc.vector.bn_stats(stats[:], y_t[:]))
                done(nc.vector.bn_aggr(mean_var[:], stats[:]))
                dve.sem_inc(var_ready, 1)
                dve.wait_ge(std_ready, t + 1)
                done(nc.vector.reciprocal(rstd[:], std[:]))
                done(nc.vector.scalar_tensor_tensor(shift[:], mean_var[:, 0:1], -1.0, rstd[:], ALU.mult, ALU.mult))
                dve.sem_inc(scale_ready, 1)

        @block.tensor
        def _(pe):
            pe.wait_ge(weights_landed, 32)
            pe.wait_ge(consts_ready, 5)
            with pe.Fori(0, TILES) as t:
                pe.wait_ge(x_landed, 16 * (t + 1))
                pe.wait_ge(agg_ready, t + 1)
                for k in range(K):
                    src = x_t if k < K // 2 else agg
                    c = (k % (K // 2)) * P
                    last = nc.tensor.transpose(h_ps[:, k, :], src[:, c:c + P], identity[:])
                last.then_inc(transposed, 1)
                pe.wait_ge(h_ready, t + 1)
                for k in range(K):
                    nc.tensor.matmul(lin_ps[:], h_T[:, k, :], w_t[:, k, :], start=(k == 0), stop=False)
                nc.tensor.matmul(lin_ps[:], ones_row[0:1, :], b_row[0:1, :], start=False, stop=True).then_inc(linear_ready, 1)

        @block.scalar
        def _(act):
            with act.Fori(0, TILES) as t:
                act.wait_ge(transposed, t + 1)
                nc.scalar.copy(h_T[:], h_ps[:]).then_inc(h_ready, 1)
                act.wait_ge(linear_ready, t + 1)
                nc.scalar.activation(relu_t[:], lin_ps[:], ACT.Relu).then_inc(relu_ready, 1)
                act.wait_ge(var_ready, t + 1)
                nc.scalar.activation(std[:], mean_var[:, 1:2], ACT.Sqrt, bias=eps_t[:, 0:1]).then_inc(std_ready, 1)
                act.wait_ge(scale_ready, t + 2)
                nc.scalar.activation(out_t[:], y_t[:], ACT.Identity, bias=shift[:, 0:1], scale=rstd[:, 0:1]).then_inc(out_ready, 1)


_INS = ["x", "adj", "L0_gnn_W", "L0_gnn_b"]


def kernel(**inputs):
    import numpy as _np
    import concourse.bacc as _bacc
    from concourse import mybir as _mybir
    from concourse.bass_utils import run_bass_kernel_spmd as _run

    nc = _bacc.Bacc("TRN2", target_bir_lowering=False, num_devices=1)
    arrays, args = {}, []
    for name in _INS:
        a = _np.ascontiguousarray(inputs[name])
        arrays[f"in_{name}"] = a
        args.append(nc.dram_tensor(f"in_{name}", a.shape, _mybir.dt.from_np(a.dtype), kind="ExternalInput").ap())
    shape = inputs["x"].shape
    args.append(nc.dram_tensor("out_0", shape, _mybir.dt.float32, kind="ExternalOutput").ap())
    graph_layer(nc, *args)
    r = _run(nc, [arrays], core_ids=[0])
    return r.results[0]["out_0"]
```

```python
from contextlib import ExitStack

import concourse.bass as bass
from concourse import mybir

P = 128
ALU = mybir.AluOpType
ACT = mybir.ActivationFunctionType
AX_X = mybir.AxisListType.X
BF16 = mybir.dt.bfloat16
F16 = mybir.dt.float16
F32 = mybir.dt.float32
I32 = mybir.dt.int32
U32 = mybir.dt.uint32

S = 25
SLOTS = 6
WORD = 16
QUARTERS = 4
PARTS = 3
UNROLL = 4
RANKS = 32
RING = 5
EPS = 1e-5
LOWEST = -3.4028234663852886e38

TRANSPOSE, PREFIX, FETCH, EXTRAS, MERGE, PROJECT, NORM, SCALE, STORE = 1, 2, 3, 4, 6, 7, 8, 9, 10
AHEAD = 13
LEAD = 3
WARM = 12


def graph_layer(nc, x, adj, w, b, out):
    B, N, C = x.shape
    TILES = B * N // P
    CHUNKS = N // P
    CPQ = CHUNKS // QUARTERS
    GROUPS = N // WORD
    GPC = P // WORD
    K = 2 * C // P
    x_rows = x.rearrange("b n c -> (b n) c")
    x_tiles = x.rearrange("b (t p) c -> (b t) p c", p=P)
    adj_tiles = adj.rearrange("b (t p) m -> (b t) p m", p=P)
    out_tiles = out.rearrange("b (t p) c -> (b t) p c", p=P)

    with ExitStack() as ctx:
        def sb(name, shape, dt=F32):
            return ctx.enter_context(nc.sbuf_tensor(name, shape, dt))

        def ps(name, shape, dt=F32):
            return ctx.enter_context(nc.psum_tensor(name, shape, dt))

        def sem(name):
            return ctx.enter_context(nc.semaphore(name))

        adj_t = sb("adj_t", [P, 4, N], I32)
        sign_t = sb("sign_t", [P, 2, N], BF16)
        mask_T = sb("mask_T", [P, 4, CHUNKS, P], BF16)
        first_T = sb("first_T", [P, 4, CHUNKS, P], BF16)
        extra_T = sb("extra_T", [P, 2, CHUNKS, P], BF16)
        top_words = sb("top_words", [P, 2, 8], I32)
        group_id = sb("group_id", [P, 2, 8], I32)
        bits = sb("bits", [P, 2, 8, WORD], I32)
        column = sb("column", [P, 2, 8, WORD])
        found = sb("found", [P, 2, 8, WORD])
        extras = sb("extras", [P, 4, 8])
        valid = sb("valid", [P, 4, 8])
        offset = sb("offset", [P, 2, 8])
        index = sb("index", [P, 4, 8], U32)
        gathered = sb("gathered", [P, 2, SLOTS, C])
        part_max = sb("part_max", [P, 2, QUARTERS, C])
        half_max = sb("half_max", [P, 2, C])
        chunk_max = sb("chunk_max", [P, 4, C])
        merged = sb("merged", [P, 2, C])
        agg = sb("agg", [P, 2, C])
        x_t = sb("x_t", [P, 4, C])
        h_T = sb("h_T", [P, 2, K, P])
        y_t = sb("y_t", [P, 4, C])
        stats = sb("stats", [P, 2, 6])
        mean_var = sb("mean_var", [P, 4, 2])
        std = sb("std", [P, 4])
        rstd = sb("rstd", [P, 4])
        shift = sb("shift", [P, 4])
        out_t = sb("out_t", [P, 2, C])
        x_live = sb("x_live", [P, CHUNKS, PARTS, C], BF16)
        x_next = sb("x_next", [P, CHUNKS, PARTS, C], BF16)
        x_ahead = sb("x_ahead", [P, 4, C])
        x_rest = sb("x_rest", [P, C])
        iota_i = sb("iota_i", [P, P], I32)
        ident_f = sb("ident_f", [P, P])
        ident_b = sb("ident_b", [P, P], BF16)
        first_w = sb("first_w", [P, P], BF16)
        word_i = sb("word_i", [P, GPC], I32)
        word_a = sb("word_a", [P, GPC])
        word_b = sb("word_b", [P, GPC])
        word_w = sb("word_w", [P, GPC], BF16)
        bit_of = sb("bit_of", [P, WORD], I32)
        place = sb("place", [P, WORD])
        group_row = sb("group_row", [1, GROUPS], BF16)
        ones_b = sb("ones_b", [1, P], BF16)
        ones_f = sb("ones_f", [1, P])
        ones_col = sb("ones_col", [P, 1])
        w_t = sb("w_t", [P, K, C])
        b_row = sb("b_row", [1, C])
        eps_t = sb("eps_t", [P, 1])
        own_i = sb("own_i", [P, UNROLL], I32)
        local_i = sb("local_i", [P, UNROLL], I32)
        own_f = sb("own_f", [P, UNROLL])
        local_f = sb("local_f", [P, UNROLL])
        crowded = sb("crowded", [P, 1])
        crowded_i = sb("crowded_i", [1, 1], I32)
        descending = sb("descending", [P, N], F16)
        ranks = sb("ranks", [P, RANKS], F16)
        g_valid = sb("g_valid", [P, S])
        g_offset = sb("g_offset", [P, 2, S])
        g_index = sb("g_index", [P, S], U32)
        floor = sb("floor", [P, 1])
        from_end = sb("from_end", [P, 1])

        mask_ps = ps("mask_ps", [P, 8, P], BF16)
        prefix_ps = ps("prefix_ps", [P, CPQ, P])
        fetch_ps = ps("fetch_ps", [P, 2, CPQ, C])
        words_ps = ps("words_ps", [P, 512])
        h_ps = ps("h_ps", [P, K, P])

        consts_landed = sem("consts_landed")
        pool_consts = sem("pool_consts")
        dve_consts = sem("dve_consts")
        sp_gate = sem("sp_gate")
        pool_gate = sem("pool_gate")
        dve_gate = sem("dve_gate")
        pe_gate = sem("pe_gate")
        adj_landed = [sem(f"adj_landed_{r}") for r in range(4)]
        ahead_landed = [sem(f"ahead_landed_{r}") for r in range(4)]
        x_landed = [sem(f"x_landed_{r}") for r in range(4)]
        rows_landed = [sem(f"rows_landed_{r}") for r in range(2)]
        out_stored = [sem(f"out_stored_{r}") for r in range(2)]
        signed = sem("signed")
        mask_full = sem("mask_full")
        mask_ready = sem("mask_ready")
        prefix_full = sem("prefix_full")
        first_ready = sem("first_ready")
        fetch_full = sem("fetch_full")
        fetch_read = sem("fetch_read")
        extra_ready = sem("extra_ready")
        words_full = sem("words_full")
        words_read = sem("words_read")
        index_ready = sem("index_ready")
        agg_ready = sem("agg_ready")
        h_full = sem("h_full")
        h_ready = sem("h_ready")
        linear_full = sem("linear_full")
        y_ready = sem("y_ready")
        var_ready = sem("var_ready")
        std_ready = sem("std_ready")
        scale_ready = sem("scale_ready")
        out_ready = sem("out_ready")
        split_done = sem("split_done")
        split_chain = sem("split_chain")
        x_copied = sem("x_copied")
        dve_chain = sem("dve_chain")
        flag_summed = sem("flag_summed")
        flag_ready = sem("flag_ready")
        g_desc = sem("g_desc")
        g_adj_landed = sem("g_adj_landed")
        g_x_landed = sem("g_x_landed")
        g_adj_used = sem("g_adj_used")
        g_index_ready = sem("g_index_ready")
        g_row_landed = [sem(f"g_row_landed_{r}") for r in range(RING)]
        g_rows_free = sem("g_rows_free")
        g_agg_ready = sem("g_agg_ready")
        g_transposed = sem("g_transposed")
        g_h_ready = sem("g_h_ready")
        g_linear_ready = sem("g_linear_ready")
        g_relu_ready = sem("g_relu_ready")
        g_var_ready = sem("g_var_ready")
        g_std_ready = sem("g_std_ready")
        g_scale_ready = sem("g_scale_ready")
        g_out_ready = sem("g_out_ready")
        g_out_stored = sem("g_out_stored")
        block = ctx.enter_context(nc.Block())

        def wait(eng, s, value, gate=None):
            if isinstance(value, int):
                if value > 0:
                    eng.wait_ge(s, value)
            else:
                eng.wait_ge(s, value)
                if gate is not None:
                    eng.sem_inc(gate, 1)

        def run_steps(eng, step):
            for s in range(WARM):
                step(s, s % UNROLL)
            with eng.Fori(WARM // UNROLL, TILES // UNROLL) as g:
                for u in range(UNROLL):
                    step(g * UNROLL + u, u)
            for s in range(TILES, TILES + STORE + 1):
                step(s, s % UNROLL)

        def alive(t):
            return not isinstance(t, int) or 0 <= t < TILES

        def turn(t, u, lag, ring):
            r = (u - lag) % ring
            return r, ((t - r) // ring + 1) if isinstance(t, int) else None

        def landed(eng, sems, t, u, lag, per=16, gate=None):
            ring = len(sems)
            r = (u - lag) % ring
            if isinstance(t, int):
                eng.wait_ge(sems[r], per * (t // ring + 1))
            else:
                wait(eng, sems[r], (t - r) * (per // ring) + per, gate)

        def dram(ap, t):
            if isinstance(t, int):
                return ap[t]
            return ap[bass.ds(t, 1), :, :].rearrange("a p m -> (a p) m")

        def load_ahead(sp, a, r):
            t = a % TILES if isinstance(a, int) else a & (TILES - 1)
            wait(sp, split_done, a - 3, sp_gate)
            sp.dma_start(x_ahead[:, r, :], dram(x_tiles, t)).then_inc(ahead_landed[r], 16)

        @block.sync
        def _(sp):
            def load_adj(t, r):
                wait(sp, signed, t - 3, sp_gate)
                sp.dma_start(adj_t[:, r, :], dram(adj_tiles, t)).then_inc(adj_landed[r], 16)

            for a in range(4):
                load_ahead(sp, a, a)
            load_adj(0, 0)
            sp.dma_start(w_t[:], w.rearrange("(k p) n -> p k n", p=P)).then_inc(consts_landed, 16)
            sp.dma_start(b_row[:], b.rearrange("(a n) -> a n", a=1)).then_inc(consts_landed, 16)
            for t in range(1, LEAD):
                load_adj(t, t)
            for a in range(4, AHEAD + 1):
                load_ahead(sp, a, a % 4)

            def step(s, u):
                if isinstance(s, int) and s >= TILES:
                    pass
                else:
                    if not (isinstance(s, int) and s + LEAD >= TILES):
                        pass
                t = s + LEAD
                if alive(t) and not isinstance(t, int) or isinstance(t, int) and t < TILES:
                    load_adj(t, (u + LEAD) % 4)
                a = s + AHEAD + 1
                if not isinstance(s, int) or s < TILES:
                    load_ahead(sp, a, (u + AHEAD + 1) % 4)
                t = s - (PROJECT - 2)
                if alive(t):
                    wait(sp, y_ready, t - 3, sp_gate)
                    r = (u - (PROJECT - 2)) % 4
                    sp.dma_start(x_t[:, r, :], dram(x_tiles, t)).then_inc(x_landed[r], 16)
                t = s - STORE
                if alive(t):
                    wait(sp, out_ready, t + 1, sp_gate)
                    r = (u - STORE) % 2
                    sp.dma_start(dram(out_tiles, t), out_t[:, r, :]).then_inc(out_stored[r], 16)

            for s in range(WARM):
                step(s, s % UNROLL)
            with sp.Fori(WARM // UNROLL, TILES // UNROLL - 1) as g:
                for u in range(UNROLL):
                    step(g * UNROLL + u, u)
            for s in range(TILES - UNROLL, TILES + STORE + 1):
                step(s, s % UNROLL)
            for r in range(2):
                sp.wait_ge(out_stored[r], 16 * TILES // 2)

            sp.wait_ge(flag_ready, 1)
            flag = sp.value_load(crowded_i[0:1, 0:1], min_val=0, max_val=1)
            with sp.If(flag > 0):
                with sp.Fori(0, TILES) as t:
                    wait(sp, g_adj_used, t + 1, sp_gate)
                    sp.dma_start(adj_t[:, 0, :], dram(adj_tiles, t)).then_inc(g_adj_landed, 16)
                    wait(sp, g_scale_ready, t + 1, sp_gate)
                    sp.dma_start(x_t[:, 0, :], dram(x_tiles, t)).then_inc(g_x_landed, 16)
                    wait(sp, g_out_ready, t + 1, sp_gate)
                    sp.dma_start(dram(out_tiles, t), out_t[:, 0, :]).then_inc(g_out_stored, 16)
                    wait(sp, g_out_stored, 16 * (t + 1), sp_gate)

        @block.gpsimd
        def _(pool):
            chain = [0]

            def done(ins):
                chain[0] += 1
                ins.then_inc(pool_gate, 1)
                pool.wait_ge(pool_gate, chain[0])

            G = nc.gpsimd
            G.memset(ident_f[:], 0.0).then_inc(pool_gate, 1)
            G.memset(word_a[:], 0.0).then_inc(pool_gate, 1)
            G.memset(ones_f[:], 1.0)
            G.memset(ones_b[:], 1.0)
            G.memset(ones_col[:], 1.0)
            G.memset(crowded[:], 0.0)
            G.memset(eps_t[:], EPS)
            chain[0] = 2
            pool.wait_ge(pool_gate, 2)
            done(G.affine_select(out=ident_f[:], in_=ident_f[:], compare_op=ALU.not_equal, fill=1.0, base=0,
                                 pattern=[[-1, P]], channel_multiplier=1))
            done(G.iota(iota_i[:], [[1, P]], base=0, channel_multiplier=-1))
            done(G.iota(word_i[:], [[-WORD, GPC]], base=0, channel_multiplier=1))
            done(G.iota(bits[:, 0, 0, :], [[1, WORD]], base=0, channel_multiplier=0))
            done(G.iota(bits[:, 1, :, :], [[1, GROUPS]], base=0, channel_multiplier=0))
            done(G.iota(own_i[:], [[P, UNROLL]], base=-2 * UNROLL * P, channel_multiplier=1))
            G.drain().then_inc(pool_consts, 1)
            split = [0]

            def split_chunk(a, u):
                r = (u + AHEAD) % 4 if u is not None else None
                if u is None:
                    r = a % 4
                c = a % CHUNKS if isinstance(a, int) else a & (CHUNKS - 1)
                dst = x_next[:, c] if isinstance(c, int) else x_next[:, bass.ds(c, 1)].rearrange("p a k f -> p (a k) f")
                if isinstance(a, int):
                    pool.wait_ge(ahead_landed[r], 16 * (a // 4 + 1))
                    wait(pool, x_copied, a // CHUNKS * QUARTERS)
                else:
                    wait(pool, ahead_landed[r], (a - r) * 4 + 16, pool_gate)
                    wait(pool, x_copied, (a >> 4) * QUARTERS, pool_gate)
                pool.sem_clear(split_chain)
                src = x_ahead[:, r, :]
                G.tensor_copy(dst[:, 0, :], src).then_inc(split_chain, 1)
                pool.wait_ge(split_chain, 1)
                G.tensor_tensor(x_rest[:], src, dst[:, 0, :], ALU.subtract).then_inc(split_chain, 1)
                pool.wait_ge(split_chain, 2)
                G.tensor_copy(dst[:, 1, :], x_rest[:]).then_inc(split_chain, 1)
                pool.wait_ge(split_chain, 3)
                G.tensor_tensor(dst[:, 2, :], x_rest[:], dst[:, 1, :], ALU.subtract).then_inc(split_chain, 1)
                pool.wait_ge(split_chain, 4)
                pool.sem_inc(split_done, 1)

            for a in range(AHEAD):
                split_chunk(a, None)

            def step(s, u):
                if not isinstance(s, int) or s < TILES:
                    split_chunk(s + AHEAD, u)
                t = s - EXTRAS
                if alive(t):
                    wait(pool, index_ready, t + 1, pool_gate)
                    wait(pool, agg_ready, t - 1, pool_gate)
                    r = (u - EXTRAS) % 2
                    for j in range(SLOTS):
                        G.indirect_dma_start(
                            out=gathered[:, r, j, :], out_offset=None, in_=x_rows[:, :],
                            in_offset=bass.IndirectOffsetOnAxis(ap=index[:, (u - EXTRAS) % 4, j:j + 1], axis=0),
                        ).then_inc(rows_landed[r], 16)

            run_steps(pool, step)

            pool.wait_ge(flag_ready, 1)
            flag = pool.value_load(crowded_i[0:1, 0:1], min_val=0, max_val=1)
            with pool.If(flag > 0):
                G.iota(adj_t[:, 1, :], [[-1, N]], base=N, channel_multiplier=0).then_inc(g_desc, 1)
                G.iota(own_i[:, 0:1], [[0, 1]], base=-P, channel_multiplier=1).then_inc(g_desc, 1)
                with pool.Fori(0, TILES) as t:
                    wait(pool, g_index_ready, t + 1, pool_gate)
                    for j in range(S):
                        wait(pool, g_rows_free, t * S + (j + 1), pool_gate)
                        G.indirect_dma_start(
                            out=gathered[:, 0, j % RING, :], out_offset=None, in_=x_rows[:, :],
                            in_offset=bass.IndirectOffsetOnAxis(ap=g_index[:, j:j + 1], axis=0),
                        ).then_inc(g_row_landed[j % RING], 16)

        @block.vector
        def _(dve):
            V = nc.vector
            count = [0]

            def done(ins):
                count[0] += 1
                ins.then_inc(dve_chain, 1)
                return count[0]

            def need(n):
                dve.wait_ge(dve_chain, n)

            dve.wait_ge(pool_consts, 1)
            done(V.tensor_copy(ident_b[:], ident_f[:]))
            need(done(V.tensor_scalar(found[:, 0].rearrange("p a b -> p (a b)"), iota_i[:], 0.0, -2.0, ALU.is_gt, ALU.mult)))
            done(V.tensor_tensor(first_w[:], found[:, 0].rearrange("p a b -> p (a b)"), ident_f[:], ALU.add))
            need(done(V.tensor_scalar(bits[:, 0, 1, :], bits[:, 0, 0, :], 0, None, ALU.bitwise_and)))
            need(done(V.tensor_scalar(bits[:, 0, 1, :], bits[:, 0, 1, :], GROUPS, None, ALU.bitwise_or)))
            need(done(V.tensor_tensor(bit_of[:], bits[:, 0, 1, :], bits[:, 0, 0, :], ALU.logical_shift_left)))
            done(V.tensor_scalar(place[:], bits[:, 0, 0, :], 1.0, None, ALU.add))
            need(done(V.tensor_copy(group_row[0:1, :], bits[0:1, 1].rearrange("p a b -> p (a b)"))))
            need(done(V.tensor_copy(word_b[:], word_i[:])))
            for j in range(WORD):
                need(done(V.tensor_scalar(column[:, 0, 0, 0:GPC], word_b[:], float(j), float(GROUPS << j), ALU.is_equal, ALU.mult)))
                need(done(V.tensor_tensor(word_a[:], word_a[:], column[:, 0, 0, 0:GPC], ALU.add)))
            need(done(V.tensor_copy(word_w[:], word_a[:])))
            dve.sem_inc(dve_consts, 1)

            def copy_features(t):
                wait(dve, split_done, t + CHUNKS, dve_gate)
                for q in range(QUARTERS):
                    V.tensor_copy(x_live[:, q * CPQ:(q + 1) * CPQ], x_next[:, q * CPQ:(q + 1) * CPQ]).then_inc(x_copied, 1)

            def step(s, u):
                if u == 0:
                    if count[0]:
                        need(count[0])
                        dve.sem_clear(dve_chain)
                        count[0] = 0
                    need(done(V.tensor_scalar(own_i[:], own_i[:], UNROLL * P, None, ALU.add)))
                    done(V.tensor_copy(own_f[:], own_i[:]))
                    need(done(V.tensor_scalar(local_i[:], own_i[:], N - 1, None, ALU.bitwise_and)))
                    need(done(V.tensor_scalar(local_f[:], local_i[:], 1.0, None, ALU.add)))

                t = s - NORM
                if alive(t):
                    r4, r2 = (u - NORM) % 4, (u - NORM) % 2
                    wait(dve, scale_ready, t - 3) if False else None
                    wait(dve, out_ready, t - 3, dve_gate)
                    wait(dve, linear_full, t + 1)
                    n = done(V.scalar_tensor_tensor(y_t[:, r4, :], h_ps.ap().rearrange("p k n -> p (k n)")[:, 0:C], 0.0,
                                                    x_t[:, r4, :], ALU.max, ALU.add))
                    need(n)
                    dve.sem_inc(y_ready, 1)
                    need(done(V.bn_stats(stats[:, r2, :], y_t[:, r4, :])))
                    V.bn_aggr(mean_var[:, r4, :], stats[:, r2, :]).then_inc(var_ready, 1)

                t = s - FETCH
                if alive(t):
                    r4, r2 = (u - FETCH) % 4, (u - FETCH) % 2
                    wait(dve, words_full, t - 1, dve_gate)
                    wait(dve, first_ready, QUARTERS * (t + 1))
                    V.tensor_tensor(extra_T[:, r2], mask_T[:, r4], first_T[:, r4], ALU.subtract).then_inc(extra_ready, 1)
                    if u == FETCH % UNROLL:
                        if isinstance(t, int):
                            if t % CHUNKS == 0:
                                copy_features(t)
                        else:
                            with dve.If((t & (CHUNKS - 1)) == 0):
                                copy_features(t)

                t = s - EXTRAS
                if alive(t):
                    r4, r2 = (u - EXTRAS) % 4, (u - EXTRAS) % 2
                    wait(dve, words_full, t + 1, dve_gate)
                    n = done(V.max(top_words[:, r2, :], words_ps[:, 0:GROUPS]))
                    need(n)
                    dve.sem_inc(words_read, 1)
                    n1 = done(V.tensor_scalar(group_id[:, r2, :], top_words[:, r2, :], GROUPS - 1, None, ALU.bitwise_and))
                    n2 = done(V.tensor_tensor(bits[:, r2], top_words[:, r2, :].unsqueeze(2).to_broadcast([P, 8, WORD]),
                                              bit_of[:].unsqueeze(1).to_broadcast([P, 8, WORD]), ALU.bitwise_and))
                    need(n1)
                    n3 = done(V.scalar_tensor_tensor(column[:, r2], group_id[:, r2, :].unsqueeze(2).to_broadcast([P, 8, WORD]),
                                                     float(WORD), place[:].unsqueeze(1).to_broadcast([P, 8, WORD]),
                                                     ALU.mult, ALU.add))
                    need(n3)
                    n4 = done(V.scalar_tensor_tensor(found[:, r2], bits[:, r2], 0.0, column[:, r2], ALU.is_gt, ALU.mult))
                    need(n4)
                    n5 = done(V.max(extras[:, r4, :], found[:, r2].rearrange("p a b -> p (a b)")))
                    need(n5)
                    done(V.tensor_tensor(crowded[:], crowded[:], extras[:, r4, SLOTS:SLOTS + 1], ALU.max))
                    col = (u - EXTRAS) % UNROLL
                    need(done(V.tensor_scalar(valid[:, r4, :], extras[:, r4, :], 0.0, None, ALU.is_gt)))
                    need(done(V.scalar_tensor_tensor(offset[:, r2, :], extras[:, r4, :], local_f[:, col:col + 1],
                                                     valid[:, r4, :], ALU.subtract, ALU.mult)))
                    V.tensor_scalar(index[:, r4, :], offset[:, r2, :], own_f[:, col:col + 1], None, ALU.add).then_inc(index_ready, 1)

                t = s - FETCH
                if alive(t):
                    r4, r2 = (u - FETCH) % 4, (u - FETCH) % 2
                    for q in range(QUARTERS):
                        wait(dve, fetch_full, QUARTERS * t + (q + 1))
                        n = done(V.tensor_reduce(part_max[:, r2, q, :], fetch_ps[:, q % 2].rearrange("p c f -> p f c"),
                                                 AX_X, ALU.max))
                        need(n)
                        dve.sem_inc(fetch_read, 1)
                    need(done(V.scalar_tensor_tensor(half_max[:], part_max[:, r2, 0:2, :], 0.0, part_max[:, r2, 2:4, :],
                                                     ALU.max, ALU.max)))
                    done(V.tensor_tensor(chunk_max[:, r4, :], half_max[:, 0, :], half_max[:, 1, :], ALU.max))

                t = s - MERGE
                if alive(t):
                    r4, r2 = (u - MERGE) % 4, (u - MERGE) % 2
                    wait(dve, h_full, t - 1, dve_gate)
                    landed(dve, rows_landed, t, u, MERGE, per=16 * SLOTS, gate=dve_gate)
                    have = chunk_max[:, r4, :]
                    for j in range(SLOTS):
                        to = agg[:, r2, :] if j == SLOTS - 1 else merged[:, j % 2, :]
                        n = done(V.scalar_tensor_tensor(to, gathered[:, r2, j, :], valid[:, r4, j:j + 1], have, ALU.mult, ALU.max))
                        need(n)
                        have = to
                    dve.sem_inc(agg_ready, 1)

                t = s - SCALE
                if alive(t):
                    r4 = (u - SCALE) % 4
                    wait(dve, std_ready, t + 1)
                    need(done(V.reciprocal(rstd[:, r4:r4 + 1], std[:, r4:r4 + 1])))
                    V.scalar_tensor_tensor(shift[:, r4:r4 + 1], mean_var[:, r4, 0:1], -1.0, rstd[:, r4:r4 + 1],
                                           ALU.mult, ALU.mult).then_inc(scale_ready, 1)

            for s in range(EXTRAS):
                step_u = s % UNROLL
                step(s, step_u)
            for s in range(EXTRAS, WARM):
                step(s, s % UNROLL)
            with dve.Fori(WARM // UNROLL, TILES // UNROLL) as g:
                for u in range(UNROLL):
                    step(g * UNROLL + u, u)
            for s in range(TILES, TILES + STORE + 1):
                step(s, s % UNROLL)
            need(count[0])

            dve.sem_inc(flag_ready, 0) if False else None
            dve.sem_clear(dve_chain)
            count[0] = 0
            dve.sem_inc(flag_summed, 1)
            dve.wait_ge(flag_summed, 2)
            V.tensor_scalar(crowded_i[:], words_ps[0:1, 0:1], 0.0, None, ALU.is_gt).then_inc(flag_ready, 1)
            dve.wait_ge(flag_ready, 1)
            flag = dve.value_load(crowded_i[0:1, 0:1], min_val=0, max_val=1)
            with dve.If(flag > 0):
                key = extra_T[:, 0].rearrange("p c n -> p (c n)").bitcast(F16)
                own, local = own_i[:, 0:1], local_i[:, 0:1]
                dve.wait_ge(g_desc, 2)
                need(done(V.tensor_copy(descending[:], adj_t[:, 1, :])))
                dve.sem_inc(g_adj_used, 1)
                dve.sem_inc(g_scale_ready, 1)
                dve.sem_inc(g_rows_free, RING)
                with dve.Fori(0, TILES) as t:
                    dve.sem_clear(dve_chain)
                    count[0] = 0
                    need(done(V.tensor_scalar(own, own, P, None, ALU.add)))
                    need(done(V.tensor_copy(own_f[:, 0:1], own)))
                    need(done(V.tensor_scalar(local, own, N - 1, None, ALU.bitwise_and)))
                    need(done(V.tensor_scalar(from_end[:], local, -1.0, float(N), ALU.mult, ALU.add)))
                    wait(dve, g_adj_landed, 16 * (t + 1))
                    need(done(V.scalar_tensor_tensor(key, adj_t[:, 0, :], 0.0, descending[:], ALU.not_equal, ALU.mult)))
                    dve.sem_inc(g_adj_used, 1)
                    for r in range(0, RANKS, 8):
                        need(done(V.max(ranks[:, r:r + 8], key)))
                        if r + 8 < RANKS:
                            need(done(V.match_replace(key, ranks[:, r:r + 8], key, 0.0)))
                    need(done(V.tensor_scalar(g_valid[:], ranks[:, 0:S], 0.0, None, ALU.is_gt)))
                    need(done(V.tensor_scalar(g_offset[:, 0], ranks[:, 0:S], -1.0, from_end[:, 0:1], ALU.mult, ALU.add)))
                    need(done(V.tensor_tensor(g_offset[:, 1], g_offset[:, 0], g_valid[:], ALU.mult)))
                    need(done(V.tensor_scalar(g_index[:], g_offset[:, 1], own_f[:, 0:1], None, ALU.add)))
                    dve.sem_inc(g_index_ready, 1)
                    need(done(V.tensor_scalar(floor[:], ranks[:, S:S + 1], 0.0, LOWEST, ALU.is_gt, ALU.mult)))
                    for j in range(S):
                        wait(dve, g_row_landed[j % RING], t * (16 * S // RING) + 16 * (j // RING + 1))
                        if j == 0:
                            need(done(V.tensor_scalar(agg[:, 0, :], gathered[:, 0, 0, :], g_valid[:, 0:1], floor[:, 0:1],
                                                      ALU.mult, ALU.max)))
                        else:
                            need(done(V.scalar_tensor_tensor(agg[:, 0, :], gathered[:, 0, j % RING, :], g_valid[:, j:j + 1],
                                                             agg[:, 0, :], ALU.mult, ALU.max)))
                        dve.sem_inc(g_rows_free, 1)
                    dve.sem_inc(g_agg_ready, 1)
                    wait(dve, g_relu_ready, t + 1)
                    need(done(V.tensor_tensor(y_t[:, 0, :], half_max[:, 0, :], x_t[:, 0, :], ALU.add)))
                    need(done(V.bn_stats(stats[:, 0, :], y_t[:, 0, :])))
                    need(done(V.bn_aggr(mean_var[:, 0, :], stats[:, 0, :])))
                    dve.sem_inc(g_var_ready, 1)
                    wait(dve, g_std_ready, t + 1)
                    need(done(V.reciprocal(rstd[:, 0:1], std[:, 0:1])))
                    need(done(V.scalar_tensor_tensor(shift[:, 0:1], mean_var[:, 0, 0:1], -1.0, rstd[:, 0:1], ALU.mult, ALU.mult)))
                    dve.sem_inc(g_scale_ready, 1)

        @block.tensor
        def _(pe):
            T = nc.tensor
            pe.wait_ge(pool_consts, 1)
            pe.wait_ge(dve_consts, 1)
            pe.wait_ge(consts_landed, 32)
            linear = h_ps.ap().rearrange("p k n -> p (k n)")[:, 0:C]

            def step(s, u):
                t = s - EXTRAS
                if alive(t):
                    r2 = (u - EXTRAS) % 2
                    wait(pe, words_read, t, pe_gate)
                    wait(pe, extra_ready, t + 1)
                    for c in range(CHUNKS):
                        T.matmul(words_ps[:, c * GPC:(c + 1) * GPC], extra_T[:, r2, c, :], word_w[:], start=(c == 0), stop=False,
                                 skip_group_check=True)
                    T.matmul(words_ps[:, 0:GROUPS], ones_b[0:1, :], group_row[0:1, :], start=False, stop=True,
                             skip_group_check=True).then_inc(words_full, 1)
                t = s - PROJECT
                if alive(t):
                    r4, r2 = (u - PROJECT) % 4, (u - PROJECT) % 2
                    landed(pe, x_landed, t, u, PROJECT, gate=pe_gate)
                    wait(pe, y_ready, t, pe_gate)
                    wait(pe, agg_ready, t + 1, pe_gate)
                    for k in range(K):
                        src = x_t[:, r4, :] if k < K // 2 else agg[:, r2, :]
                        c = (k % (K // 2)) * P
                        last = T.transpose(h_ps[:, k, :], src[:, c:c + P], ident_f[:])
                    last.then_inc(h_full, 1)
                for q in range(QUARTERS):
                    t = s - TRANSPOSE
                    if alive(t):
                        if q == 0:
                            wait(pe, signed, t + 1, pe_gate)
                        wait(pe, mask_ready, QUARTERS * t + q, pe_gate)
                        for c in range(q * CPQ, (q + 1) * CPQ):
                            last = T.transpose(mask_ps[:, c - q * CPQ, :], sign_t[:, (u - TRANSPOSE) % 2, c * P:(c + 1) * P], ident_b[:])
                        last.then_inc(mask_full, 1)
                    t = s - PREFIX
                    if alive(t):
                        wait(pe, first_ready, QUARTERS * t + q, pe_gate)
                        wait(pe, mask_ready, QUARTERS * t + (q + 1))
                        T.matmul(prefix_ps[:], first_w[:], mask_T[:, (u - PREFIX) % 4, q * CPQ:(q + 1) * CPQ, :],
                                 start=True, stop=True).then_inc(prefix_full, 1)
                    t = s - FETCH
                    if alive(t):
                        wait(pe, x_copied, (t // CHUNKS if isinstance(t, int) else (t >> 4)) * QUARTERS + (q + 1), pe_gate)
                        wait(pe, fetch_read, QUARTERS * t + (q - 1), pe_gate)
                        wait(pe, first_ready, QUARTERS * t + (q + 1))
                        for c in range(q * CPQ, (q + 1) * CPQ):
                            for k in range(PARTS):
                                last = T.matmul(fetch_ps[:, q % 2, c - q * CPQ, :], first_T[:, (u - FETCH) % 4, c, :],
                                                x_live[:, c, k, :], start=(k == 0), stop=(k == PARTS - 1))
                        last.then_inc(fetch_full, 1)
                    t = s - PROJECT
                    if alive(t) and q == 2:
                        wait(pe, h_ready, t + 1, pe_gate)
                        for k in range(K):
                            T.matmul(linear, h_T[:, (u - PROJECT) % 2, k, :], w_t[:, k, :], start=(k == 0), stop=False)
                        T.matmul(linear, ones_f[0:1, :], b_row[0:1, :], start=False, stop=True).then_inc(linear_full, 1)

            run_steps(pe, step)
            pe.wait_ge(flag_summed, 1)
            T.matmul(words_ps[0:1, 0:1], crowded[:, 0:1], ones_col[:, 0:1], start=True, stop=True).then_inc(flag_summed, 1)
            pe.wait_ge(flag_ready, 1)
            flag = pe.value_load(crowded_i[0:1, 0:1], min_val=0, max_val=1)
            with pe.If(flag > 0):
                with pe.Fori(0, TILES) as t:
                    wait(pe, g_x_landed, 16 * (t + 1), pe_gate)
                    wait(pe, g_agg_ready, t + 1, pe_gate)
                    for k in range(K):
                        src = x_t[:, 0, :] if k < K // 2 else agg[:, 0, :]
                        c = (k % (K // 2)) * P
                        last = T.transpose(h_ps[:, k, :], src[:, c:c + P], ident_f[:])
                    last.then_inc(g_transposed, 1)
                    wait(pe, g_h_ready, t + 1, pe_gate)
                    for k in range(K):
                        T.matmul(linear, h_T[:, 0, k, :], w_t[:, k, :], start=(k == 0), stop=False)
                    T.matmul(linear, ones_f[0:1, :], b_row[0:1, :], start=False, stop=True).then_inc(g_linear_ready, 1)

        @block.scalar
        def _(act):
            A = nc.scalar
            act.wait_ge(pool_consts, 1)
            linear = h_ps.ap().rearrange("p k n -> p (k n)")[:, 0:C]

            def step(s, u):
                t = s
                if alive(t):
                    r = u % 4
                    wait(act, mask_full, QUARTERS * (t - 1))
                    landed(act, adj_landed, t, u, 0)
                    A.activation(sign_t[:, u % 2, :], adj_t[:, r, :], ACT.Sign).then_inc(signed, 1)
                for q in range(QUARTERS):
                    t = s - TRANSPOSE
                    if alive(t):
                        if q == 0:
                            wait(act, extra_ready, t - 3)
                        wait(act, mask_full, QUARTERS * t + (q + 1))
                        A.activation(mask_T[:, (u - TRANSPOSE) % 4, q * CPQ:(q + 1) * CPQ, :], mask_ps[:, 0:CPQ, :],
                                     ACT.Abs).then_inc(mask_ready, 1)
                    t = s - PREFIX
                    if alive(t):
                        if q == 0:
                            wait(act, fetch_full, QUARTERS * (t - 3))
                        wait(act, prefix_full, QUARTERS * t + (q + 1))
                        A.activation(first_T[:, (u - PREFIX) % 4, q * CPQ:(q + 1) * CPQ, :], prefix_ps[:],
                                     ACT.Relu).then_inc(first_ready, 1)
                    t = s - PROJECT
                    if alive(t) and q == 0:
                        wait(act, linear_full, t - 1)
                        wait(act, h_full, t + 1)
                        A.copy(h_T[:, (u - PROJECT) % 2], h_ps[:]).then_inc(h_ready, 1)
                t = s - NORM
                if alive(t):
                    r4 = (u - NORM) % 4
                    wait(act, var_ready, t + 1)
                    A.activation(std[:, r4:r4 + 1], mean_var[:, r4, 1:2], ACT.Sqrt, bias=eps_t[:, 0:1]).then_inc(std_ready, 1)
                t = s - SCALE
                if alive(t):
                    r4, r2 = (u - SCALE) % 4, (u - SCALE) % 2
                    if not isinstance(t, int):
                        wait(act, out_stored[r2], (t - r2) * 8)
                    elif t >= 2:
                        act.wait_ge(out_stored[r2], 16 * (t // 2))
                    wait(act, scale_ready, t + 1)
                    A.activation(out_t[:, r2, :], y_t[:, r4, :], ACT.Identity, bias=shift[:, r4:r4 + 1],
                                 scale=rstd[:, r4:r4 + 1]).then_inc(out_ready, 1)

            run_steps(act, step)
            act.wait_ge(flag_ready, 1)
            flag = act.value_load(crowded_i[0:1, 0:1], min_val=0, max_val=1)
            with act.If(flag > 0):
                for r in range(2):
                    act.wait_ge(out_stored[r], 16 * TILES // 2)
                with act.Fori(0, TILES) as t:
                    wait(act, g_transposed, t + 1)
                    A.copy(h_T[:, 0], h_ps[:]).then_inc(g_h_ready, 1)
                    wait(act, g_linear_ready, t + 1)
                    A.activation(half_max[:, 0, :], linear, ACT.Relu).then_inc(g_relu_ready, 1)
                    wait(act, g_var_ready, t + 1)
                    A.activation(std[:, 0:1], mean_var[:, 0, 1:2], ACT.Sqrt, bias=eps_t[:, 0:1]).then_inc(g_std_ready, 1)
                    wait(act, g_scale_ready, t + 2)
                    A.activation(out_t[:, 0, :], y_t[:, 0, :], ACT.Identity, bias=shift[:, 0:1],
                                 scale=rstd[:, 0:1]).then_inc(g_out_ready, 1)


_INS = ["x", "adj", "L0_gnn_W", "L0_gnn_b"]


def kernel(**inputs):
    import numpy as _np
    import concourse.bacc as _bacc
    from concourse import mybir as _mybir
    from concourse.bass_utils import run_bass_kernel_spmd as _run

    nc = _bacc.Bacc("TRN2", target_bir_lowering=False, num_devices=1)
    arrays, args = {}, []
    for name in _INS:
        a = _np.ascontiguousarray(inputs[name])
        arrays[f"in_{name}"] = a
        args.append(nc.dram_tensor(f"in_{name}", a.shape, _mybir.dt.from_np(a.dtype), kind="ExternalInput").ap())
    shape = inputs["x"].shape
    args.append(nc.dram_tensor("out_0", shape, _mybir.dt.float32, kind="ExternalOutput").ap())
    graph_layer(nc, *args)
    r = _run(nc, [arrays], core_ids=[0])
    return r.results[0]["out_0"]
```

```python
from contextlib import ExitStack

import concourse.bass as bass
from concourse import mybir

P = 128
ALU = mybir.AluOpType
ACT = mybir.ActivationFunctionType
AX_X = mybir.AxisListType.X
BF16 = mybir.dt.bfloat16
F16 = mybir.dt.float16
F32 = mybir.dt.float32
I32 = mybir.dt.int32
U32 = mybir.dt.uint32

S = 25
SLOTS = 5
WORD = 16
QUARTERS = 4
PARTS = 3
UNROLL = 4
RANKS = 32
RING = 5
EPS = 1e-5
LOWEST = -3.4028234663852886e38

TRANSPOSE, PREFIX, FETCH, EXTRAS, MERGE, PROJECT, LINEAR, RESIDUAL, NORM, SCALE, STORE = 1, 2, 3, 4, 6, 7, 8, 8, 9, 10, 11
AHEAD = 13
LEAD = 3
WARM = 12


def graph_layer(nc, x, adj, w, b, out):
    B, N, C = x.shape
    TILES = B * N // P
    CHUNKS = N // P
    CPQ = CHUNKS // QUARTERS
    PAIRS = CHUNKS // 2
    GROUPS = N // WORD
    GPC = P // WORD
    K = 2 * C // P
    x_rows = x.rearrange("b n c -> (b n) c")
    x_tiles = x.rearrange("b (t p) c -> (b t) p c", p=P)
    adj_tiles = adj.rearrange("b (t p) m -> (b t) p m", p=P)
    out_tiles = out.rearrange("b (t p) c -> (b t) p c", p=P)

    with ExitStack() as ctx:
        def sb(name, shape, dt=F32):
            return ctx.enter_context(nc.sbuf_tensor(name, shape, dt))

        def ps(name, shape, dt=F32):
            return ctx.enter_context(nc.psum_tensor(name, shape, dt))

        def sem(name):
            return ctx.enter_context(nc.semaphore(name))

        adj_t = sb("adj_t", [P, 4, N], I32)
        sign_t = sb("sign_t", [P, 2, N], BF16)
        mask_T = sb("mask_T", [P, 4, CHUNKS, P], BF16)
        first_T = sb("first_T", [P, 4, CHUNKS, P], BF16)
        g_key = sb("g_key", [P, N], F16)
        top_words = sb("top_words", [P, 2, 8], I32)
        group_id = sb("group_id", [P, 2, 8], I32)
        bits = sb("bits", [P, 2, 8, WORD], I32)
        column = sb("column", [P, 2, 8, WORD])
        found = sb("found", [P, 2, 8, WORD])
        extras = sb("extras", [P, 4, 8])
        valid = sb("valid", [P, 4, 8])
        distance = sb("distance", [P, 2, 8])
        offset = sb("offset", [P, 2, 8])
        index = sb("index", [P, 4, 8], U32)
        gathered = sb("gathered", [P, 4, SLOTS, C])
        pair_max = sb("pair_max", [P, 2, 2, C])
        chunk_max = sb("chunk_max", [P, 4, C])
        merged = sb("merged", [P, 2, C])
        agg = sb("agg", [P, 2, C])
        x_t = sb("x_t", [P, 4, C])
        h_T = sb("h_T", [P, 2, K, P])
        relu_t = sb("relu_t", [P, 2, C])
        y_t = sb("y_t", [P, 4, C])
        stats = sb("stats", [P, 2, 6])
        mean_var = sb("mean_var", [P, 4, 2])
        std = sb("std", [P, 4])
        rstd = sb("rstd", [P, 4])
        shift = sb("shift", [P, 4])
        out_t = sb("out_t", [P, 2, C])
        x_parts = sb("x_parts", [P, 2 * CHUNKS, PARTS, C], BF16)
        x_ahead = sb("x_ahead", [P, 4, C])
        x_rest = sb("x_rest", [P, 2, C])
        iota_i = sb("iota_i", [P, P], I32)
        ident_f = sb("ident_f", [P, P])
        ident_b = sb("ident_b", [P, P], BF16)
        first_w = sb("first_w", [P, P], BF16)
        word_i = sb("word_i", [P, GPC], I32)
        word_a = sb("word_a", [P, GPC])
        word_b = sb("word_b", [P, GPC])
        word_bit = sb("word_bit", [P, 2, GPC])
        word_w = sb("word_w", [P, GPC], BF16)
        word_less = sb("word_less", [P, GPC], BF16)
        bit_of = sb("bit_of", [P, WORD], I32)
        place = sb("place", [P, WORD])
        group_row = sb("group_row", [1, GROUPS], BF16)
        ones_b = sb("ones_b", [1, P], BF16)
        ones_b3 = sb("ones_b3", [PARTS, P], BF16)
        b_split = sb("b_split", [1, PARTS, C], BF16)
        b_rest = sb("b_rest", [1, C])
        b_parts = sb("b_parts", [PARTS, C], BF16)
        ones_col = sb("ones_col", [P, 1])
        w_t = sb("w_t", [P, K, C])
        b_row = sb("b_row", [1, C])
        eps_t = sb("eps_t", [P, 1])
        own_i = sb("own_i", [P, UNROLL], I32)
        own_f = sb("own_f", [P, UNROLL])
        local_f = sb("local_f", [P, UNROLL])
        wrap_f = sb("wrap_f", [P, UNROLL])
        local_i = sb("local_i", [P, 1], I32)
        crowded = sb("crowded", [P, 1])
        crowded_i = sb("crowded_i", [1, 1], I32)
        descending = sb("descending", [P, N], F16)
        ranks = sb("ranks", [P, RANKS], F16)
        g_valid = sb("g_valid", [P, S])
        g_offset = sb("g_offset", [P, 2, S])
        g_index = sb("g_index", [P, S], U32)
        floor = sb("floor", [P, 1])
        from_end = sb("from_end", [P, 1])

        mask_ps = ps("mask_ps", [P, 8, P], BF16)
        prefix_ps = ps("prefix_ps", [P, CPQ, P])
        fetch_ps = ps("fetch_ps", [P, 4, 2, C])
        words_ps = ps("words_ps", [P, 512])
        h_ps = ps("h_ps", [P, K, P])

        consts_landed = sem("consts_landed")
        bias_spread = sem("bias_spread")
        pool_consts = sem("pool_consts")
        dve_consts = sem("dve_consts")
        sp_gate = sem("sp_gate")
        pool_gate = sem("pool_gate")
        dve_gate = sem("dve_gate")
        act_gate = sem("act_gate")
        pe_gate = sem("pe_gate")
        adj_landed = [sem(f"adj_landed_{r}") for r in range(4)]
        ahead_landed = [sem(f"ahead_landed_{r}") for r in range(4)]
        x_landed = [sem(f"x_landed_{r}") for r in range(4)]
        rows_landed = [sem(f"rows_landed_{r}") for r in range(4)]
        out_stored = [sem(f"out_stored_{r}") for r in range(2)]
        signed = sem("signed")
        mask_full = sem("mask_full")
        mask_ready = sem("mask_ready")
        prefix_full = sem("prefix_full")
        first_ready = sem("first_ready")
        fetch_full = sem("fetch_full")
        fetch_read = sem("fetch_read")
        words_full = sem("words_full")
        words_read = sem("words_read")
        extras_ready = sem("extras_ready")
        pool_chain = sem("pool_chain")
        agg_ready = sem("agg_ready")
        h_full = sem("h_full")
        h_ready = sem("h_ready")
        linear_full = sem("linear_full")
        relu_ready = sem("relu_ready")
        y_ready = sem("y_ready")
        var_ready = sem("var_ready")
        std_ready = sem("std_ready")
        scale_ready = sem("scale_ready")
        out_ready = sem("out_ready")
        split_done = sem("split_done")
        high_ready = sem("high_ready")
        rest_ready = sem("rest_ready")
        mid_ready = sem("mid_ready")
        dve_chain = sem("dve_chain")
        flag_summed = sem("flag_summed")
        flag_ready = sem("flag_ready")
        g_desc = sem("g_desc")
        g_adj_landed = sem("g_adj_landed")
        g_x_landed = sem("g_x_landed")
        g_adj_used = sem("g_adj_used")
        g_index_ready = sem("g_index_ready")
        g_row_landed = [sem(f"g_row_landed_{r}") for r in range(RING)]
        g_rows_free = sem("g_rows_free")
        g_agg_ready = sem("g_agg_ready")
        g_transposed = sem("g_transposed")
        g_h_ready = sem("g_h_ready")
        g_linear_ready = sem("g_linear_ready")
        g_relu_ready = sem("g_relu_ready")
        g_var_ready = sem("g_var_ready")
        g_std_ready = sem("g_std_ready")
        g_scale_ready = sem("g_scale_ready")
        g_out_ready = sem("g_out_ready")
        g_out_stored = sem("g_out_stored")
        block = ctx.enter_context(nc.Block())

        def wait(eng, s, value, gate=None):
            if isinstance(value, int):
                if value > 0:
                    eng.wait_ge(s, value)
            else:
                eng.wait_ge(s, value)
                if gate is not None:
                    eng.sem_inc(gate, 1)

        def run_steps(eng, step):
            for s in range(WARM):
                step(s, s % UNROLL)
            with eng.Fori(WARM // UNROLL, TILES // UNROLL) as g:
                for u in range(UNROLL):
                    step(g * UNROLL + u, u)
            for s in range(TILES, TILES + STORE + 1):
                step(s, s % UNROLL)

        def alive(t):
            return not isinstance(t, int) or 0 <= t < TILES

        def turn(t, u, lag, ring):
            r = (u - lag) % ring
            return r, ((t - r) // ring + 1) if isinstance(t, int) else None

        def landed(eng, sems, t, u, lag, per=16, gate=None):
            ring = len(sems)
            r = (u - lag) % ring
            if isinstance(t, int):
                eng.wait_ge(sems[r], per * (t // ring + 1))
            else:
                wait(eng, sems[r], (t - r) * (per // ring) + per, gate)

        def dram(ap, t):
            if isinstance(t, int):
                return ap[t]
            return ap[bass.ds(t, 1), :, :].rearrange("a p m -> (a p) m")

        def part_of(a, k):
            if isinstance(a, int):
                return x_parts[:, a % (2 * CHUNKS), k, :]
            return x_parts[:, bass.ds(a & (2 * CHUNKS - 1), 1), k, :].rearrange("p a f -> p (a f)")

        def rest_of(eng, a, r):
            gate = pool_gate if eng is nc.gpsimd else None
            wait(eng, split_done, a - 1, gate)
            wait(eng, high_ready, a + 1, gate)
            eng.tensor_tensor(x_rest[:, r % 2, :], x_ahead[:, r, :], part_of(a, 0), ALU.subtract).then_inc(rest_ready, 1)

        def low_of(eng, a, r):
            gate = pool_gate if eng is nc.gpsimd else None
            wait(eng, mid_ready, a + 1, gate)
            eng.tensor_tensor(part_of(a, 2), x_rest[:, r % 2, :], part_of(a, 1), ALU.subtract).then_inc(split_done, 1)

        def load_ahead(sp, a, r):
            t = a % TILES if isinstance(a, int) else a & (TILES - 1)
            wait(sp, rest_ready, a - 3, sp_gate)
            sp.dma_start(x_ahead[:, r, :], dram(x_tiles, t)).then_inc(ahead_landed[r], 16)

        @block.sync
        def _(sp):
            def load_adj(t, r):
                wait(sp, signed, QUARTERS * (t - 3), sp_gate)
                sp.dma_start(adj_t[:, r, :], dram(adj_tiles, t)).then_inc(adj_landed[r], 16)

            for a in range(4):
                load_ahead(sp, a, a)
            load_adj(0, 0)
            sp.dma_start(w_t[:], w.rearrange("(k p) n -> p k n", p=P)).then_inc(consts_landed, 16)
            sp.dma_start(b_row[:], b.rearrange("(a n) -> a n", a=1)).then_inc(consts_landed, 16)
            for a in range(4, AHEAD + 1):
                load_ahead(sp, a, a % 4)
                if a % 4 == 0 and a // 4 < LEAD:
                    load_adj(a // 4, a // 4)
            sp.wait_ge(pool_consts, 2)
            sp.dma_start(b_parts[:], b_split[:]).then_inc(bias_spread, 16)

            def step(s, u):
                t = s + LEAD
                if alive(t):
                    load_adj(t, (u + LEAD) % 4)
                a = s + AHEAD + 1
                if not isinstance(s, int) or s < TILES:
                    load_ahead(sp, a, (u + AHEAD + 1) % 4)
                t = s - (PROJECT - 2)
                if alive(t):
                    wait(sp, y_ready, t - 3, sp_gate)
                    r = (u - (PROJECT - 2)) % 4
                    sp.dma_start(x_t[:, r, :], dram(x_tiles, t)).then_inc(x_landed[r], 16)
                t = s - STORE
                if alive(t):
                    wait(sp, out_ready, t + 1, sp_gate)
                    r = (u - STORE) % 2
                    sp.dma_start(dram(out_tiles, t), out_t[:, r, :]).then_inc(out_stored[r], 16)

            for s in range(WARM):
                step(s, s % UNROLL)
            with sp.Fori(WARM // UNROLL, TILES // UNROLL - 1) as g:
                for u in range(UNROLL):
                    step(g * UNROLL + u, u)
            for s in range(TILES - UNROLL, TILES + STORE + 1):
                step(s, s % UNROLL)
            for r in range(2):
                sp.wait_ge(out_stored[r], 16 * TILES // 2)

            sp.wait_ge(flag_ready, 1)
            flag = sp.value_load(crowded_i[0:1, 0:1], min_val=0, max_val=1)
            with sp.If(flag > 0):
                with sp.Fori(0, TILES) as t:
                    wait(sp, g_adj_used, t + 1, sp_gate)
                    sp.dma_start(adj_t[:, 0, :], dram(adj_tiles, t)).then_inc(g_adj_landed, 16)
                    wait(sp, g_scale_ready, t + 1, sp_gate)
                    sp.dma_start(x_t[:, 0, :], dram(x_tiles, t)).then_inc(g_x_landed, 16)
                    wait(sp, g_out_ready, t + 1, sp_gate)
                    sp.dma_start(dram(out_tiles, t), out_t[:, 0, :]).then_inc(g_out_stored, 16)
                    wait(sp, g_out_stored, 16 * (t + 1), sp_gate)

        @block.gpsimd
        def _(pool):
            chain = [0]

            def done(ins):
                chain[0] += 1
                ins.then_inc(pool_gate, 1)
                pool.wait_ge(pool_gate, chain[0])

            G = nc.gpsimd
            G.memset(ident_f[:], 0.0).then_inc(pool_gate, 1)
            G.memset(word_a[:], 0.0).then_inc(pool_gate, 1)
            G.memset(ones_b3[:], 1.0)
            G.memset(ones_b[:], 1.0)
            G.memset(ones_col[:], 1.0)
            G.memset(crowded[:], 0.0)
            G.memset(eps_t[:], EPS)
            chain[0] = 2
            pool.wait_ge(pool_gate, 2)
            done(G.affine_select(out=ident_f[:], in_=ident_f[:], compare_op=ALU.not_equal, fill=1.0, base=0,
                                 pattern=[[-1, P]], channel_multiplier=1))
            done(G.iota(iota_i[:], [[1, P]], base=0, channel_multiplier=-1))
            done(G.iota(word_i[:], [[-WORD, GPC]], base=0, channel_multiplier=1))
            done(G.iota(bits[:, 0, 0, :], [[1, WORD]], base=0, channel_multiplier=0))
            done(G.iota(bits[:, 1, :, :], [[1, GROUPS]], base=0, channel_multiplier=0))
            done(G.iota(own_i[:], [[P, UNROLL]], base=-UNROLL * P, channel_multiplier=1))
            done(G.tensor_copy(own_f[:], own_i[:]))
            done(G.tensor_scalar(local_f[:], own_i[:], 1.0, None, ALU.add))
            G.drain().then_inc(pool_consts, 1)
            done(G.tensor_copy(word_b[:], word_i[:]))
            for j in range(WORD):
                done(G.tensor_scalar(word_bit[:, j % 2, :], word_b[:], float(j), float(GROUPS << j), ALU.is_equal, ALU.mult))
                done(G.tensor_tensor(word_a[:], word_a[:], word_bit[:, j % 2, :], ALU.add))
            done(G.tensor_copy(word_w[:], word_a[:]))
            done(G.tensor_scalar(word_less[:], word_a[:], -1.0, None, ALU.mult))
            pool.wait_ge(consts_landed, 32)
            done(G.tensor_copy(b_split[:, 0, :], b_row[:]))
            done(G.tensor_tensor(b_rest[:], b_row[:], b_split[:, 0, :], ALU.subtract))
            done(G.tensor_copy(b_split[:, 1, :], b_rest[:]))
            done(G.tensor_tensor(b_split[:, 2, :], b_rest[:], b_split[:, 1, :], ALU.subtract))
            pool.sem_inc(pool_consts, 1)

            pool.wait_ge(split_done, AHEAD)

            def step(s, u):
                if not isinstance(s, int) or s < TILES:
                    rest_of(nc.gpsimd, s + AHEAD, (u + AHEAD) % 4)
                    low_of(nc.gpsimd, s + AHEAD, (u + AHEAD) % 4)
                t = s - EXTRAS
                if alive(t):
                    r, r2 = (u - EXTRAS) % 4, (u - EXTRAS) % 2
                    if u == 0:
                        pool.sem_clear(pool_chain)
                        G.tensor_scalar(own_f[:], own_f[:], float(UNROLL * P), None, ALU.add).then_inc(pool_chain, 1)
                        G.tensor_scalar(local_f[:], local_f[:], float(UNROLL * P), None, ALU.add).then_inc(pool_chain, 1)
                        pool.wait_ge(pool_chain, 2)
                        G.tensor_scalar(wrap_f[:], local_f[:], float(N), float(-N), ALU.is_gt, ALU.mult).then_inc(pool_chain, 1)
                        pool.wait_ge(pool_chain, 3)
                        G.tensor_tensor(local_f[:], local_f[:], wrap_f[:], ALU.add).then_inc(pool_chain, 1)
                        pool.wait_ge(pool_chain, 4)
                    n = 4 * (u + 1)
                    wait(pool, extras_ready, t + 1, pool_gate)
                    wait(pool, agg_ready, t - 3, pool_gate)
                    G.tensor_scalar(valid[:, r, :], extras[:, r, :], 0.0, None, ALU.is_gt).then_inc(pool_chain, 1)
                    G.tensor_scalar(distance[:, r2, :], extras[:, r, :], local_f[:, u:u + 1], None, ALU.subtract).then_inc(pool_chain, 1)
                    G.tensor_tensor(crowded[:], crowded[:], extras[:, r, SLOTS:SLOTS + 1], ALU.add)
                    pool.wait_ge(pool_chain, n + 2)
                    G.tensor_tensor(offset[:, r2, :], distance[:, r2, :], valid[:, r, :], ALU.mult).then_inc(pool_chain, 1)
                    pool.wait_ge(pool_chain, n + 3)
                    G.tensor_scalar(index[:, r, :], offset[:, r2, :], own_f[:, u:u + 1], None, ALU.add).then_inc(pool_chain, 1)
                    pool.wait_ge(pool_chain, n + 4)
                    for j in range(SLOTS):
                        G.indirect_dma_start(
                            out=gathered[:, r, j, :], out_offset=None, in_=x_rows[:, :],
                            in_offset=bass.IndirectOffsetOnAxis(ap=index[:, (u - EXTRAS) % 4, j:j + 1], axis=0),
                        ).then_inc(rows_landed[r], 16)
                t = s - RESIDUAL
                if alive(t):
                    r4 = (u - RESIDUAL) % 4
                    wait(pool, out_ready, t - 3, pool_gate)
                    landed(pool, x_landed, t, u, RESIDUAL, gate=pool_gate)
                    wait(pool, relu_ready, t + 1)
                    G.tensor_tensor(y_t[:, r4, :], relu_t[:, (u - RESIDUAL) % 2, :], x_t[:, r4, :], ALU.add).then_inc(y_ready, 1)

            run_steps(pool, step)
            G.drain().then_inc(flag_summed, 1)

            pool.wait_ge(flag_ready, 1)
            flag = pool.value_load(crowded_i[0:1, 0:1], min_val=0, max_val=1)
            with pool.If(flag > 0):
                G.iota(adj_t[:, 1, :], [[-1, N]], base=N, channel_multiplier=0).then_inc(g_desc, 1)
                G.iota(own_i[:, 0:1], [[0, 1]], base=-P, channel_multiplier=1).then_inc(g_desc, 1)
                with pool.Fori(0, TILES) as t:
                    wait(pool, g_index_ready, t + 1, pool_gate)
                    for j in range(S):
                        wait(pool, g_rows_free, t * S + (j + 1), pool_gate)
                        G.indirect_dma_start(
                            out=gathered[:, 0, j % RING, :], out_offset=None, in_=x_rows[:, :],
                            in_offset=bass.IndirectOffsetOnAxis(ap=g_index[:, j:j + 1], axis=0),
                        ).then_inc(g_row_landed[j % RING], 16)

        @block.vector
        def _(dve):
            V = nc.vector
            count = [0]

            def done(ins):
                count[0] += 1
                ins.then_inc(dve_chain, 1)
                return count[0]

            def need(n):
                dve.wait_ge(dve_chain, n)

            dve.wait_ge(pool_consts, 1)
            done(V.tensor_copy(ident_b[:], ident_f[:]))
            need(done(V.tensor_scalar(found[:, 0].rearrange("p a b -> p (a b)"), iota_i[:], 0.0, -2.0, ALU.is_gt, ALU.mult)))
            done(V.tensor_tensor(first_w[:], found[:, 0].rearrange("p a b -> p (a b)"), ident_f[:], ALU.add))
            need(done(V.tensor_scalar(bits[:, 0, 1, :], bits[:, 0, 0, :], 0, None, ALU.bitwise_and)))
            need(done(V.tensor_scalar(bits[:, 0, 1, :], bits[:, 0, 1, :], GROUPS, None, ALU.bitwise_or)))
            need(done(V.tensor_tensor(bit_of[:], bits[:, 0, 1, :], bits[:, 0, 0, :], ALU.logical_shift_left)))
            done(V.tensor_scalar(place[:], bits[:, 0, 0, :], 1.0, None, ALU.add))
            need(done(V.tensor_copy(group_row[0:1, :], bits[0:1, 1].rearrange("p a b -> p (a b)"))))
            dve.sem_inc(dve_consts, 1)

            def restart():
                need(count[0])
                dve.sem_clear(dve_chain)
                count[0] = 0

            restart()

            rest_of(nc.vector, 0, 0)
            for a in range(AHEAD):
                if a + 1 < AHEAD:
                    rest_of(nc.vector, a + 1, (a + 1) % 4)
                wait(dve, rest_ready, a + 1)
                V.tensor_copy(part_of(a, 1), x_rest[:, a % 2, :]).then_inc(mid_ready, 1)
                low_of(nc.vector, a, a % 4)

            def step(s, u):
                fetch, words, merge, norm, scale = s - FETCH, s - EXTRAS, s - MERGE, s - NORM, s - SCALE
                f4, e4, e2, m4, m2 = (u - FETCH) % 4, (u - EXTRAS) % 4, (u - EXTRAS) % 2, (u - MERGE) % 4, (u - MERGE) % 2
                n4, n2, s4 = (u - NORM) % 4, (u - NORM) % 2, (u - SCALE) % 4
                step_of = {}

                def chunk_pair(i):
                    if alive(fetch):
                        wait(dve, fetch_full, PAIRS * fetch + (i + 1))
                        to, new = pair_max[:, i % 2], fetch_ps[:, i % 4]
                        if i == 0:
                            ins = V.tensor_scalar(to, new, 0.0, None, ALU.max)
                        else:
                            wait(dve, fetch_read, PAIRS * fetch + i)
                            ins = V.tensor_tensor(to, new, pair_max[:, (i - 1) % 2], ALU.max)
                        ins.then_inc(fetch_read, 1)

                def merge_slot(j):
                    if alive(merge):
                        if j == 0:
                            landed(dve, rows_landed, merge, u, MERGE, per=16 * SLOTS)
                        else:
                            need(step_of["merge", j - 1])
                        have = chunk_max[:, m4, :] if j == 0 else merged[:, (j - 1) % 2, :]
                        to = agg[:, m2, :] if j == SLOTS - 1 else merged[:, j % 2, :]
                        if j == SLOTS - 1:
                            wait(dve, h_full, merge - 1, dve_gate)
                        ins = V.scalar_tensor_tensor(to, gathered[:, m4, j, :], valid[:, m4, j:j + 1], have, ALU.mult, ALU.max)
                        if j == SLOTS - 1:
                            ins.then_inc(agg_ready, 1)
                        else:
                            step_of["merge", j] = done(ins)

                chunk_pair(0)
                if alive(words):
                    wait(dve, words_full, words + 1, dve_gate)
                    V.max(top_words[:, e2, :], words_ps[:, 0:GROUPS]).then_inc(words_read, 1)
                merge_slot(0)
                chunk_pair(1)
                if alive(words):
                    wait(dve, words_read, words + 1)
                    a = done(V.tensor_scalar(group_id[:, e2, :], top_words[:, e2, :], GROUPS - 1, None, ALU.bitwise_and))
                    done(V.tensor_tensor(bits[:, e2], top_words[:, e2, :].unsqueeze(2).to_broadcast([P, 8, WORD]),
                                         bit_of[:].unsqueeze(1).to_broadcast([P, 8, WORD]), ALU.bitwise_and))
                merge_slot(1)
                if alive(words):
                    need(a)
                    c = done(V.scalar_tensor_tensor(column[:, e2], group_id[:, e2, :].unsqueeze(2).to_broadcast([P, 8, WORD]),
                                                    float(WORD), place[:].unsqueeze(1).to_broadcast([P, 8, WORD]),
                                                    ALU.mult, ALU.add))
                chunk_pair(2)
                merge_slot(2)
                if alive(words):
                    need(c)
                    f = done(V.scalar_tensor_tensor(found[:, e2], bits[:, e2], 0.0, column[:, e2], ALU.is_gt, ALU.mult))
                chunk_pair(3)
                if alive(words):
                    need(f)
                    V.max(extras[:, e4, :], found[:, e2].rearrange("p a b -> p (a b)")).then_inc(extras_ready, 1)
                chunk_pair(4)
                merge_slot(3)
                chunk_pair(5)
                merge_slot(4)
                if alive(norm):
                    wait(dve, y_ready, norm + 1)
                    n = done(V.bn_stats(stats[:, n2, :], y_t[:, n4, :]))
                chunk_pair(6)
                if alive(norm):
                    need(n)
                    V.bn_aggr(mean_var[:, n4, :], stats[:, n2, :]).then_inc(var_ready, 1)
                if alive(scale):
                    wait(dve, std_ready, scale + 1)
                    r = done(V.reciprocal(rstd[:, s4:s4 + 1], std[:, s4:s4 + 1]))
                chunk_pair(7)
                if alive(scale):
                    need(r)
                    V.scalar_tensor_tensor(shift[:, s4:s4 + 1], mean_var[:, s4, 0:1], -1.0, rstd[:, s4:s4 + 1],
                                           ALU.mult, ALU.mult).then_inc(scale_ready, 1)
                if alive(fetch):
                    last = pair_max[:, (PAIRS - 1) % 2]
                    wait(dve, fetch_read, PAIRS * (fetch + 1))
                    done(V.tensor_tensor(chunk_max[:, f4, :], last[:, 0, :], last[:, 1, :], ALU.max))
                if u == UNROLL - 1:
                    restart()

            run_steps(dve, step)
            restart()

            dve.sem_inc(flag_summed, 1)
            dve.wait_ge(flag_summed, 3)
            V.tensor_scalar(crowded_i[:], words_ps[0:1, 0:1], 0.0, None, ALU.is_gt).then_inc(flag_ready, 1)
            dve.wait_ge(flag_ready, 1)
            flag = dve.value_load(crowded_i[0:1, 0:1], min_val=0, max_val=1)
            with dve.If(flag > 0):
                key = g_key[:]
                own, local = own_i[:, 0:1], local_i[:, 0:1]
                dve.wait_ge(g_desc, 2)
                need(done(V.tensor_copy(descending[:], adj_t[:, 1, :])))
                dve.sem_inc(g_adj_used, 1)
                dve.sem_inc(g_scale_ready, 1)
                dve.sem_inc(g_rows_free, RING)
                with dve.Fori(0, TILES) as t:
                    dve.sem_clear(dve_chain)
                    count[0] = 0
                    need(done(V.tensor_scalar(own, own, P, None, ALU.add)))
                    need(done(V.tensor_copy(own_f[:, 0:1], own)))
                    need(done(V.tensor_scalar(local, own, N - 1, None, ALU.bitwise_and)))
                    need(done(V.tensor_scalar(from_end[:], local, -1.0, float(N), ALU.mult, ALU.add)))
                    wait(dve, g_adj_landed, 16 * (t + 1))
                    need(done(V.scalar_tensor_tensor(key, adj_t[:, 0, :], 0.0, descending[:], ALU.not_equal, ALU.mult)))
                    dve.sem_inc(g_adj_used, 1)
                    for r in range(0, RANKS, 8):
                        need(done(V.max(ranks[:, r:r + 8], key)))
                        if r + 8 < RANKS:
                            need(done(V.match_replace(key, ranks[:, r:r + 8], key, 0.0)))
                    need(done(V.tensor_scalar(g_valid[:], ranks[:, 0:S], 0.0, None, ALU.is_gt)))
                    need(done(V.tensor_scalar(g_offset[:, 0], ranks[:, 0:S], -1.0, from_end[:, 0:1], ALU.mult, ALU.add)))
                    need(done(V.tensor_tensor(g_offset[:, 1], g_offset[:, 0], g_valid[:], ALU.mult)))
                    need(done(V.tensor_scalar(g_index[:], g_offset[:, 1], own_f[:, 0:1], None, ALU.add)))
                    dve.sem_inc(g_index_ready, 1)
                    need(done(V.tensor_scalar(floor[:], ranks[:, S:S + 1], 0.0, LOWEST, ALU.is_gt, ALU.mult)))
                    for j in range(S):
                        wait(dve, g_row_landed[j % RING], t * (16 * S // RING) + 16 * (j // RING + 1))
                        if j == 0:
                            need(done(V.tensor_scalar(agg[:, 0, :], gathered[:, 0, 0, :], g_valid[:, 0:1], floor[:, 0:1],
                                                      ALU.mult, ALU.max)))
                        else:
                            need(done(V.scalar_tensor_tensor(agg[:, 0, :], gathered[:, 0, j % RING, :], g_valid[:, j:j + 1],
                                                             agg[:, 0, :], ALU.mult, ALU.max)))
                        dve.sem_inc(g_rows_free, 1)
                    dve.sem_inc(g_agg_ready, 1)
                    wait(dve, g_relu_ready, t + 1)
                    need(done(V.tensor_tensor(y_t[:, 0, :], relu_t[:, 0, :], x_t[:, 0, :], ALU.add)))
                    need(done(V.bn_stats(stats[:, 0, :], y_t[:, 0, :])))
                    need(done(V.bn_aggr(mean_var[:, 0, :], stats[:, 0, :])))
                    dve.sem_inc(g_var_ready, 1)
                    wait(dve, g_std_ready, t + 1)
                    need(done(V.reciprocal(rstd[:, 0:1], std[:, 0:1])))
                    need(done(V.scalar_tensor_tensor(shift[:, 0:1], mean_var[:, 0, 0:1], -1.0, rstd[:, 0:1], ALU.mult, ALU.mult)))
                    dve.sem_inc(g_scale_ready, 1)

        @block.tensor
        def _(pe):
            T = nc.tensor
            pe.wait_ge(pool_consts, 1)
            pe.wait_ge(dve_consts, 1)
            linear = h_ps.ap().rearrange("p k n -> p (k n)")[:, 0:C]

            def step(s, u):
                t = s - FETCH
                if isinstance(t, int):
                    step_in(s, u, t // CHUNKS % 2)
                else:
                    with pe.If((t & CHUNKS) == 0):
                        step_in(s, u, 0)
                    with pe.Else():
                        step_in(s, u, 1)

            def step_in(s, u, half):
                f4 = (u - FETCH) % 4

                def word(c):
                    to = words_ps[:, c * GPC:(c + 1) * GPC]
                    T.matmul(to, mask_T[:, f4, c, :], word_w[:], start=(c == 0), stop=False, skip_group_check=True)
                    T.matmul(to, first_T[:, f4, c, :], word_less[:], start=False, stop=False, skip_group_check=True)

                for q in range(QUARTERS):
                    t = s - FETCH
                    if alive(t):
                        if isinstance(t, int):
                            wait(pe, split_done, t // CHUNKS * CHUNKS + (q + 1) * CPQ)
                        elif q == 0:
                            wait(pe, split_done, ((t >> 4) + 1) * CHUNKS, pe_gate)
                        wait(pe, first_ready, QUARTERS * t + (q + 1), pe_gate)
                        if q == QUARTERS // 2:
                            if isinstance(t, int) and t == 0:
                                pe.wait_ge(pool_consts, 2)
                                pe.wait_ge(consts_landed, 32)
                                pe.wait_ge(bias_spread, 16)
                            wait(pe, words_read, t)
                        for i in range(2 * q, 2 * q + 2):
                            wait(pe, fetch_read, PAIRS * t + (i - 3))
                            for c in range(2 * i, 2 * i + 2):
                                for k in range(PARTS):
                                    last = T.matmul(fetch_ps[:, i % 4, c % 2, :], first_T[:, f4, c, :],
                                                    x_parts[:, half * CHUNKS + c, k, :], start=(k == 0), stop=(k == PARTS - 1))
                                    if i >= PAIRS // 2 and k < 2:
                                        word(2 * c + k - CHUNKS)
                            last.then_inc(fetch_full, 1)
                        if q == QUARTERS - 1:
                            T.matmul(words_ps[:, 0:GROUPS], ones_b[0:1, :], group_row[0:1, :], start=False, stop=True,
                                     skip_group_check=True).then_inc(words_full, 1)
                    t = s - TRANSPOSE
                    if alive(t):
                        wait(pe, signed, QUARTERS * t + (q + 1), pe_gate)
                        wait(pe, mask_ready, QUARTERS * t + q)
                        for c in range(q * CPQ, (q + 1) * CPQ):
                            last = T.transpose(mask_ps[:, c - q * CPQ, :], sign_t[:, (u - TRANSPOSE) % 2, c * P:(c + 1) * P], ident_b[:])
                        last.then_inc(mask_full, 1)
                    t = s - PREFIX
                    if alive(t):
                        wait(pe, first_ready, QUARTERS * t + q, pe_gate)
                        wait(pe, mask_ready, QUARTERS * t + (q + 1))
                        T.matmul(prefix_ps[:], first_w[:], mask_T[:, (u - PREFIX) % 4, q * CPQ:(q + 1) * CPQ, :],
                                 start=True, stop=True).then_inc(prefix_full, 1)
                    t = s - PROJECT
                    if alive(t) and q == 2:
                        r4, r2 = (u - PROJECT) % 4, (u - PROJECT) % 2
                        landed(pe, x_landed, t, u, PROJECT, gate=pe_gate)
                        wait(pe, relu_ready, t, pe_gate)
                        wait(pe, agg_ready, t + 1, pe_gate)
                        for k in range(K):
                            src = x_t[:, r4, :] if k < K // 2 else agg[:, r2, :]
                            c = (k % (K // 2)) * P
                            last = T.transpose(h_ps[:, k, :], src[:, c:c + P], ident_f[:])
                        last.then_inc(h_full, 1)
                    t = s - LINEAR
                    if alive(t) and q == 0:
                        wait(pe, h_ready, t + 1, pe_gate)
                        for k in range(K):
                            T.matmul(linear, h_T[:, (u - LINEAR) % 2, k, :], w_t[:, k, :], start=(k == 0), stop=False)
                        T.matmul(linear, ones_b3[:], b_parts[:], start=False, stop=True).then_inc(linear_full, 1)

            run_steps(pe, step)
            pe.wait_ge(flag_summed, 2)
            T.matmul(words_ps[0:1, 0:1], crowded[:, 0:1], ones_col[:, 0:1], start=True, stop=True).then_inc(flag_summed, 1)
            pe.wait_ge(flag_ready, 1)
            flag = pe.value_load(crowded_i[0:1, 0:1], min_val=0, max_val=1)
            with pe.If(flag > 0):
                with pe.Fori(0, TILES) as t:
                    wait(pe, g_x_landed, 16 * (t + 1), pe_gate)
                    wait(pe, g_agg_ready, t + 1, pe_gate)
                    for k in range(K):
                        src = x_t[:, 0, :] if k < K // 2 else agg[:, 0, :]
                        c = (k % (K // 2)) * P
                        last = T.transpose(h_ps[:, k, :], src[:, c:c + P], ident_f[:])
                    last.then_inc(g_transposed, 1)
                    wait(pe, g_h_ready, t + 1, pe_gate)
                    for k in range(K):
                        T.matmul(linear, h_T[:, 0, k, :], w_t[:, k, :], start=(k == 0), stop=False)
                    T.matmul(linear, ones_b3[:], b_parts[:], start=False, stop=True).then_inc(g_linear_ready, 1)

        @block.scalar
        def _(act):
            A = nc.scalar
            act.wait_ge(pool_consts, 1)
            linear = h_ps.ap().rearrange("p k n -> p (k n)")[:, 0:C]

            def high_of(a, r):
                landed(act, ahead_landed, a, r, 0, gate=act_gate)
                if not isinstance(a, int) or a >= 2 * CHUNKS:
                    wait(act, fetch_full, PAIRS * (a - CHUNKS), act_gate)
                A.copy(part_of(a, 0), x_ahead[:, r, :]).then_inc(high_ready, 1)

            def mid_of(a, r):
                wait(act, rest_ready, a + 1, act_gate)
                A.copy(part_of(a, 1), x_rest[:, r % 2, :]).then_inc(mid_ready, 1)

            for a in range(AHEAD):
                high_of(a, a % 4)

            def step(s, u):
                for q in range(QUARTERS):
                    t = s
                    if alive(t):
                        if q == 0:
                            wait(act, mask_full, QUARTERS * (t - 1), act_gate)
                            landed(act, adj_landed, t, u, 0)
                        part = slice(q * (N // QUARTERS), (q + 1) * (N // QUARTERS))
                        A.activation(sign_t[:, u % 2, part], adj_t[:, u % 4, part], ACT.Sign).then_inc(signed, 1)
                    if not isinstance(s, int) or s < TILES:
                        if q == 0:
                            high_of(s + AHEAD, (u + AHEAD) % 4)
                        if q == 1:
                            mid_of(s + AHEAD, (u + AHEAD) % 4)
                    t = s - TRANSPOSE
                    if alive(t):
                        if q == 0:
                            wait(act, words_full, t - 3, act_gate)
                        wait(act, mask_full, QUARTERS * t + (q + 1))
                        A.activation(mask_T[:, (u - TRANSPOSE) % 4, q * CPQ:(q + 1) * CPQ, :], mask_ps[:, 0:CPQ, :],
                                     ACT.Abs).then_inc(mask_ready, 1)
                    t = s - PREFIX
                    if alive(t):
                        wait(act, prefix_full, QUARTERS * t + (q + 1))
                        A.activation(first_T[:, (u - PREFIX) % 4, q * CPQ:(q + 1) * CPQ, :], prefix_ps[:],
                                     ACT.Relu).then_inc(first_ready, 1)
                    t = s - RESIDUAL
                    if alive(t) and q == 1:
                        wait(act, y_ready, t - 1, act_gate)
                        wait(act, linear_full, t + 1)
                        A.activation(relu_t[:, (u - RESIDUAL) % 2, :], linear, ACT.Relu).then_inc(relu_ready, 1)
                    t = s - PROJECT
                    if alive(t) and q == 3:
                        wait(act, h_full, t + 1)
                        A.copy(h_T[:, (u - PROJECT) % 2], h_ps[:]).then_inc(h_ready, 1)
                t = s - NORM
                if alive(t):
                    r4 = (u - NORM) % 4
                    wait(act, var_ready, t + 1)
                    A.activation(std[:, r4:r4 + 1], mean_var[:, r4, 1:2], ACT.Sqrt, bias=eps_t[:, 0:1]).then_inc(std_ready, 1)
                t = s - SCALE
                if alive(t):
                    r4, r2 = (u - SCALE) % 4, (u - SCALE) % 2
                    if not isinstance(t, int):
                        wait(act, out_stored[r2], (t - r2) * 8)
                    elif t >= 2:
                        act.wait_ge(out_stored[r2], 16 * (t // 2))
                    wait(act, scale_ready, t + 1)
                    A.activation(out_t[:, r2, :], y_t[:, r4, :], ACT.Identity, bias=shift[:, r4:r4 + 1],
                                 scale=rstd[:, r4:r4 + 1]).then_inc(out_ready, 1)

            run_steps(act, step)
            act.wait_ge(flag_ready, 1)
            flag = act.value_load(crowded_i[0:1, 0:1], min_val=0, max_val=1)
            with act.If(flag > 0):
                for r in range(2):
                    act.wait_ge(out_stored[r], 16 * TILES // 2)
                with act.Fori(0, TILES) as t:
                    wait(act, g_transposed, t + 1)
                    A.copy(h_T[:, 0], h_ps[:]).then_inc(g_h_ready, 1)
                    wait(act, g_linear_ready, t + 1)
                    A.activation(relu_t[:, 0, :], linear, ACT.Relu).then_inc(g_relu_ready, 1)
                    wait(act, g_var_ready, t + 1)
                    A.activation(std[:, 0:1], mean_var[:, 0, 1:2], ACT.Sqrt, bias=eps_t[:, 0:1]).then_inc(g_std_ready, 1)
                    wait(act, g_scale_ready, t + 2)
                    A.activation(out_t[:, 0, :], y_t[:, 0, :], ACT.Identity, bias=shift[:, 0:1],
                                 scale=rstd[:, 0:1]).then_inc(g_out_ready, 1)


_INS = ["x", "adj", "L0_gnn_W", "L0_gnn_b"]


def kernel(**inputs):
    import numpy as _np
    import concourse.bacc as _bacc
    from concourse import mybir as _mybir
    from concourse.bass_utils import run_bass_kernel_spmd as _run

    nc = _bacc.Bacc("TRN2", target_bir_lowering=False, num_devices=1)
    arrays, args = {}, []
    for name in _INS:
        a = _np.ascontiguousarray(inputs[name])
        arrays[f"in_{name}"] = a
        args.append(nc.dram_tensor(f"in_{name}", a.shape, _mybir.dt.from_np(a.dtype), kind="ExternalInput").ap())
    shape = inputs["x"].shape
    args.append(nc.dram_tensor("out_0", shape, _mybir.dt.float32, kind="ExternalOutput").ap())
    graph_layer(nc, *args)
    r = _run(nc, [arrays], core_ids=[0])
    return r.results[0]["out_0"]
```
